# Optimizing a Trainium2 kernel written in Bass

```python
import numpy as np
import jax
import jax.numpy as jnp

def _softmax(x, axis=-1):
    return jax.nn.softmax(x, axis=axis)

def _gelu(x):
    return jax.nn.gelu(x, approximate=True)

def _silu(x):
    return jax.nn.silu(x)

def _sigmoid(x):
    return jax.nn.sigmoid(x)

def _layernorm(x, axis=-1, eps=1e-05):
    m = jnp.mean(x, axis=axis, keepdims=True)
    v = jnp.var(x, axis=axis, keepdims=True)
    return (x - m) / jnp.sqrt(v + eps)

def _scatter_add(tgt, idx, src, axis=0):
    return tgt.at[idx].add(src)

def _segment_sum(src, seg, n):
    return jax.ops.segment_sum(src, seg, n)
kernel_name = 'mk_seq_preln_d1_jaxref_r4_3ef11b'

def setup_inputs(seed: int=0):
    np.random.seed(seed)
    _w = jnp.asarray

    def _L0_attn_setup():
        import jax, jax.numpy as jnp
        import numpy as np
        HIDDEN = 1024
        NUM_HEADS = 32
        HEAD_DIM = HIDDEN // NUM_HEADS
        B, S = (2, 256)

        def _alibi_slopes(n):
            start = 2.0 ** (-2.0 ** (-(np.log2(n) - 3)))
            return np.array([start ** (i + 1) for i in range(n)], dtype=np.float32)
        key = jax.random.key(seed)
        k1, k2, k3, k4 = jax.random.split(key, 4)
        hidden_states = jax.random.normal(k1, (B, S, HIDDEN), jnp.float32)
        Wq = jax.random.normal(k2, (HIDDEN, HIDDEN), jnp.float32) * 0.02
        Wkv = jax.random.normal(k3, (HIDDEN, 2 * HEAD_DIM), jnp.float32) * 0.02
        Wo = jax.random.normal(k4, (HIDDEN, HIDDEN), jnp.float32) * 0.02
        return {'hidden_states': hidden_states, 'Wq': Wq, 'Wkv': Wkv, 'Wo': Wo}
    _L0_attn_in = _L0_attn_setup()

    def _L0_ffn_setup():
        import jax, jax.numpy as jnp
        import numpy as np
        IN_FEATURES = 1024

        def _dequantize(qweight, scale, zero_point):
            N, K_packed = qweight.shape
            groups = K_packed // 3
            p = qweight.reshape(N, groups, 3)
            v0 = p[:, :, 0] & 63
            v1 = p[:, :, 0] >> 6 & 63
            v2 = p[:, :, 1] & 63
            v3 = p[:, :, 2] & 63
            unpacked = jnp.stack([v0, v1, v2, v3], axis=2).reshape(N, groups * 4)
            unpacked = unpacked[:, :IN_FEATURES]
            return (unpacked.astype(jnp.float32) - zero_point) * scale
        key = jax.random.key(seed)
        k1, k2, k3, k4, k5 = jax.random.split(key, 5)
        x = jax.random.normal(k1, (8, 512, 1024), dtype=jnp.float32)
        qweight = jax.random.randint(k2, (1024, 768), 0, 1024, dtype=jnp.int32)
        weight_scale = jax.random.uniform(k3, (1024, 1), dtype=jnp.float32) * 0.02 + 0.001
        weight_zero_point = jax.random.uniform(k4, (1024, 1), dtype=jnp.float32) * 63.0
        bias = jax.random.normal(k5, (1024,), dtype=jnp.float32)
        return {'x': x, 'qweight': qweight, 'weight_scale': weight_scale, 'weight_zero_point': weight_zero_point, 'bias': bias}
    _L0_ffn_in = _L0_ffn_setup()
    _d = {'L0_attn_hidden_states': _L0_attn_in['hidden_states'], 'L0_attn_Wq': _L0_attn_in['Wq'], 'L0_attn_Wkv': _L0_attn_in['Wkv'], 'L0_attn_Wo': _L0_attn_in['Wo'], 'L0_ffn_qweight': _L0_ffn_in['qweight'], 'L0_ffn_weight_scale': _L0_ffn_in['weight_scale'], 'L0_ffn_weight_zero_point': _L0_ffn_in['weight_zero_point'], 'L0_ffn_bias': _L0_ffn_in['bias']}
    _x0 = _d['L0_attn_hidden_states']
    _d['L0_attn_hidden_states'] = jax.random.normal(jax.random.fold_in(jax.random.key(seed), 1), (4, 512, 1024), dtype=_x0.dtype)
    del _x0
    return _d

def reference(L0_attn_hidden_states, L0_attn_Wq, L0_attn_Wkv, L0_attn_Wo, L0_ffn_qweight, L0_ffn_weight_scale, L0_ffn_weight_zero_point, L0_ffn_bias):

    def _L0_attn_ref(hidden_states, Wq, Wkv, Wo):
        import jax, jax.numpy as jnp
        import numpy as np
        HIDDEN = 1024
        NUM_HEADS = 32
        HEAD_DIM = HIDDEN // NUM_HEADS
        B, S = (2, 256)

        def _alibi_slopes(n):
            start = 2.0 ** (-2.0 ** (-(np.log2(n) - 3)))
            return np.array([start ** (i + 1) for i in range(n)], dtype=np.float32)
        b, s, h = hidden_states.shape
        scale = HEAD_DIM ** (-0.5)
        q = (hidden_states @ Wq).reshape(b, s, NUM_HEADS, HEAD_DIM)
        kv = hidden_states @ Wkv
        k, v = (kv[..., :HEAD_DIM], kv[..., HEAD_DIM:])
        scores = jnp.einsum('bqhd,bkd->bhqk', q, k) * scale
        pos = jnp.arange(s)
        slopes = jnp.asarray(_alibi_slopes(NUM_HEADS))
        bias = slopes[:, None, None] * (pos[None, None, :] - pos[None, :, None]).astype(jnp.float32)
        causal = pos[None, :] <= pos[:, None]
        scores = jnp.where(causal[None, None], scores + bias[None], -jnp.inf)
        attn = jax.nn.softmax(scores, axis=-1)
        out = jnp.einsum('bhqk,bkd->bqhd', attn, v).reshape(b, s, h)
        return out @ Wo

    def _L0_ffn_ref(x, qweight, weight_scale, weight_zero_point, bias):
        import jax, jax.numpy as jnp
        import numpy as np
        IN_FEATURES = 1024

        def _dequantize(qweight, scale, zero_point):
            N, K_packed = qweight.shape
            groups = K_packed // 3
            p = qweight.reshape(N, groups, 3)
            v0 = p[:, :, 0] & 63
            v1 = p[:, :, 0] >> 6 & 63
            v2 = p[:, :, 1] & 63
            v3 = p[:, :, 2] & 63
            unpacked = jnp.stack([v0, v1, v2, v3], axis=2).reshape(N, groups * 4)
            unpacked = unpacked[:, :IN_FEATURES]
            return (unpacked.astype(jnp.float32) - zero_point) * scale
        w = _dequantize(qweight, weight_scale, weight_zero_point)
        return jnp.einsum('bsk,nk->bsn', x, w) + bias
    x = L0_attn_hidden_states
    x = x + _L0_attn_ref(_layernorm(x, axis=-1), L0_attn_Wq, L0_attn_Wkv, L0_attn_Wo)
    x = x + _L0_ffn_ref(_layernorm(x, axis=-1), L0_ffn_qweight, L0_ffn_weight_scale, L0_ffn_weight_zero_point, L0_ffn_bias)
    return x

_drawn_inputs = setup_inputs


def setup_inputs(seed=0):
    import zlib

    import numpy as np

    out = dict(_drawn_inputs(seed))
    spreads = {}
    factors = {}
    for name, (base, spread) in spreads.items():
        noise = np.random.default_rng([zlib.crc32(name.encode()), seed]).standard_normal(out[name].shape)
        drawn = base * np.exp(spread * noise) if base else spread * noise
        out[name] = jnp.asarray(drawn.astype(out[name].dtype))
    for name, factor in factors.items():
        out[name] = (out[name] * factor).astype(out[name].dtype)
    return out
```

```python
from contextlib import ExitStack

import concourse.bass as bass
import numpy as np
from concourse import mybir

ALU = mybir.AluOpType
ACT = mybir.ActivationFunctionType
F32 = mybir.dt.float32
F32R = mybir.dt.float32r
BF16 = mybir.dt.bfloat16
I32 = mybir.dt.int32

P = 128
B, S, D = 4, 512, 1024
HEADS, HD = 32, 32
ROWS = B * S
CK = D // P
TPB = S // P
TILES = ROWS // P
GROUPS = HEADS // 4
EPS = 1e-5
LOWEST = -3.0e38
FAR = -1.0e30
ZERO_CODE = 32.0
SCALE = float(HD) ** -0.5

R_BIAS, R_MAX, R_END = 96, 98, 100

KB_AT = (0, 512, 1024, 896)
KB_LEN = tuple(S - P * kb for kb in range(4))
PT_COLS = sum(KB_LEN)


def at_least(eng, sem, value):
    if isinstance(value, int) and value <= 0:
        return
    eng.wait_ge(sem, value)


def wait_apart(eng, sem, value, passed):
    eng.wait_ge(sem, value)
    if not isinstance(value, int):
        eng.sem_inc(passed, 1)


def project(nc, x, wq, wkv, qweight, kpos, slopes, qh_d, ql_d, ext_d, wi_d, keep):
    ident, identb, kst, vst, eps = (keep[n] for n in ("ident", "identb", "kst", "vst", "eps"))
    with ExitStack() as ctx:
        def sb(name, shape, dt=F32):
            return ctx.enter_context(nc.sbuf_tensor(name, shape, dt))

        def psum(name, shape, dt=F32):
            return ctx.enter_context(nc.psum_tensor(name, shape, dt))

        def sem(name):
            return ctx.enter_context(nc.semaphore(name))

        wqh, wql = sb("wqh", [P, CK, D], F32R), sb("wql", [P, CK, D], F32R)
        wkvh, wkvl = sb("wkvh", [P, CK, P], F32R), sb("wkvl", [P, CK, P], F32R)
        raw = sb("raw", [P, 2, 2, 512])
        raw_kv = sb("raw_kv", [P, CK, 64])
        xin = sb("xin", [P, 2, D])
        xn = sb("xn", [P, 2, D])
        xth, xtl = sb("xth", [P, 2 * CK, S], F32R), sb("xtl", [P, 2 * CK, S], F32R)
        stats = sb("stats", [P, 2, 2, 6])
        mv = sb("mv", [P, 2, 4])
        kt = sb("kt", [P, S])
        qh, ql = sb("qh", [P, 2, S], F32R), sb("ql", [P, 2, S], F32R)
        qw = sb("qw", [P, D // 4, 3], I32)
        codes = sb("codes", [P, D // 4, 4], I32)
        codes_b = sb("codes_b", [P, D], BF16)
        wt = sb("wt", [P, CK, P], F32R)
        kpos_raw = sb("kpos_raw", [P, S])
        slopes_raw, slopes_r = sb("slopes_raw", [64, S]), sb("slopes_r", [64, S], F32R)

        p_q = [psum(f"p_q{i}", [P, S]) for i in range(2)]
        p_tr = [psum(f"p_tr{i}", [P, 4, P]) for i in range(2)]
        p_kv = psum("p_kv", [P, S])
        p_vt = psum("p_vt", [P, TPB, P])
        p_w = psum("p_w", [P, CK, P], BF16)

        consts = sem("consts")
        x_in = [sem(f"x_in{i}") for i in range(2)]
        kpos_in, slopes_in, slopes_rounded, ext_out = sem("kpos_in"), sem("slopes_in"), sem("slopes_rounded"), sem("ext_out")
        raw_in = [sem(f"raw_in{i}") for i in range(2)]
        kv_in, kv_hi, kv_lo = sem("kv_in"), sem("kv_hi"), sem("kv_lo")
        wq_hi, wq_lo = sem("wq_hi"), sem("wq_lo")
        ln_stats, ln_aggr, ln_std, ln_rstd, xn_done = (sem(n) for n in ("ln_stats", "ln_aggr", "ln_std", "ln_rstd", "xn_done"))
        tr_done, tr_hi, tr_lo = sem("tr_done"), sem("tr_hi"), sem("tr_lo")
        kv_done, kt_done, k_done, vt_done, v_done = (sem(n) for n in ("kv_done", "kt_done", "k_done", "vt_done", "v_done"))
        q_done, qh_done, q_freed = sem("q_done"), sem("qh_done"), sem("q_freed")
        q_out = [sem(f"q_out{i}") for i in range(2)]
        qw_in, unpacked, codes_done, wtr_done, wt_done, wt_out = (
            sem(n) for n in ("qw_in", "unpacked", "codes_done", "wtr_done", "wt_done", "wt_out"))

        tile_after = {2: 0, 4: 1, 5: 2, 6: 3}
        tile_before = {1: 0, 3: 1, 4: 2, 5: 3}
        codes_after = {3: 0, 7: 1}
        x_rows = x.rearrange("b s d -> (b s) d")
        wq_v = wq.rearrange("(c p) n -> p c n", p=P)

        block = ctx.enter_context(nc.Block("project"))

        @block.sync
        def _(sp):
            def load_x(T, t):
                sp.dma_start(xin[:, t % 2, :], x_rows[bass.ds(T * P, P), :]).then_inc(x_in[t % 2], 16)

            def load_codes(J):
                at_least(sp, unpacked, 4 * J)
                sp.dma_start(qw[:, :, :].rearrange("p g i -> p (g i)"), qweight[bass.ds(J * P, P), :]).then_inc(qw_in, 16)

            def step(b, more):
                if more:
                    load_x(4 * b + 4, 0)
                    load_x(4 * b + 5, 1)
                load_codes(2 * b)
                for m in range(CK):
                    if more and tile_before.get(m) in (0, 1):
                        t = tile_before[m]
                        sp.wait_ge(xn_done, 4 * b + 4 + t + 1)
                        load_x(4 * b + 6 + t, t)
                    n = 8 * b + m
                    sp.wait_ge(q_freed, n + 3)
                    rows, cols = slice(m * P, (m + 1) * P), bass.ds(b * S, S)
                    sp.dma_start(qh_d[rows, cols], qh[:, m % 2, :].bitcast(F32)).then_inc(q_out[m % 2], 16)
                    sp.dma_start(ql_d[rows, cols], ql[:, m % 2, :].bitcast(F32)).then_inc(q_out[m % 2], 16)
                    if m in codes_after:
                        J = 2 * b + codes_after[m]
                        if m == 3:
                            load_codes(J + 1)
                        wait_apart(sp, wt_done, J + 1, keep["passed"])
                        sp.dma_start(wi_d[:, :, bass.ds(J * P, P)], wt[:, :, :].bitcast(F32)).then_inc(wt_out, 16)

            load_x(0, 0)
            load_x(1, 1)
            sp.dma_start(kpos_raw[R_BIAS:R_END, :], kpos).then_inc(kpos_in, 16)
            sp.dma_start(slopes_raw[:, :], slopes.rearrange("r h s -> (r h) s")).then_inc(slopes_in, 16)
            for t in range(2):
                sp.wait_ge(xn_done, t + 1)
                load_x(2 + t, t)
            sp.wait_ge(slopes_rounded, 1)
            sp.dma_start(ext_d.rearrange("r (h s) -> (r h) s", s=S), slopes_r[:, :].bitcast(F32)).then_inc(ext_out, 16)
            step(0, True)
            with sp.Fori(1, B - 1) as b:
                step(b, True)
            step(B - 1, False)
            sp.wait_ge(ext_out, 16)
            for i in range(2):
                sp.wait_ge(q_out[i], 32 * (B * CK // 2))
            sp.wait_ge(wt_out, 16 * 2 * B)

        @block.gpsimd
        def _(pool):
            pool.dma_start(raw_kv[:, :, :], wkv.rearrange("(c p) n -> p c n", p=P)).then_inc(kv_in, 16)

            def load_wq(u):
                half, c = u // 4, 2 * (u % 4)
                pool.dma_start(raw[:, u % 2, :, :], wq_v[:, c:c + 2, half * 512:(half + 1) * 512]).then_inc(raw_in[u % 2], 16)

            load_wq(0)
            load_wq(1)
            pool.memset(ident[:, :], 0.0).then_inc(consts, 1)
            pool.memset(identb[:, :], 0.0).then_inc(consts, 1)
            pool.memset(keep["ones"][:, :], 1.0).then_inc(consts, 1)
            pool.memset(keep["mask"][:, :], 0.0).then_inc(consts, 1)
            pool.memset(eps[:, :], EPS).then_inc(consts, 1)
            pool.memset(keep["future"][:, :], 0.0).then_inc(consts, 1)
            pool.wait_ge(consts, 6)
            for eye in (ident, identb):
                pool.affine_select(out=eye[:, :], in_=eye[:, :], compare_op=ALU.not_equal, fill=1.0, base=0,
                                   pattern=[[-1, P]], channel_multiplier=1).then_inc(consts, 1)
            own = keep["mask"][:, S - P:S]
            pool.affine_select(out=own, in_=own, compare_op=ALU.is_ge, fill=LOWEST, base=0,
                               pattern=[[-1, P]], channel_multiplier=1).then_inc(consts, 1)
            future = keep["future"][:, :]
            pool.affine_select(out=future, in_=future, compare_op=ALU.is_ge, fill=FAR, base=0,
                               pattern=[[1, P]], channel_multiplier=-1).then_inc(consts, 1)
            for u in range(2, 8):
                pool.wait_ge(wq_lo, u - 1)
                load_wq(u)

        @block.tensor
        def _(pe):
            def turn(T, t):
                pe.wait_ge(xn_done, T + 1)
                for half in range(2):
                    at_least(pe, tr_lo, 2 * T - 1 + half)
                    for i in range(4):
                        c = 4 * half + i
                        last = pe.transpose(p_tr[half][:, i, :], xn[:, t % 2, c * P:(c + 1) * P], ident[:, :])
                    last.then_inc(tr_done, 1)

            def passes(out, wh, wl, cols, at):
                for c in range(CK):
                    for k, (w, xt) in enumerate(((wh, xth), (wl, xth), (wh, xtl))):
                        last = pe.matmul(out, w[:, c, cols], xt[:, bass.ds(at + c, 1), :].rearrange("p a s -> p (a s)"),
                                         start=(c == 0 and k == 0), stop=(c == CK - 1 and k == 2))
                return last

            def step(b, more):
                at = (b % 2) * CK
                pe.wait_ge(tr_lo, 8 * b + 8)
                pe.wait_ge(kv_lo, 4)
                at_least(pe, kt_done, 2 * b)
                passes(p_kv[:, :], wkvh, wkvl, slice(0, P), at).then_inc(kv_done, 1)
                for m in range(CK):
                    n = 8 * b + m
                    pe.wait_ge(wq_lo, 4 if m < 4 else 8)
                    pe.wait_ge(q_freed, n + 1)
                    last = passes(p_q[m % 2][:, :], wqh, wql, slice(m * P, (m + 1) * P), at)
                    last.then_inc(q_done, 1)
                    if m == 0:
                        pe.wait_ge(kt_done, 2 * b + 2)
                        at_least(pe, v_done, b)
                        for i in range(TPB):
                            last = pe.transpose(p_vt[:, i, :], kt[:, i * P:(i + 1) * P], ident[:, :])
                        last.then_inc(vt_done, 1)
                    if more and m in tile_after:
                        turn(4 * b + 4 + tile_after[m], tile_after[m])
                    if m in codes_after:
                        J = 2 * b + codes_after[m]
                        pe.wait_ge(codes_done, J + 1)
                        at_least(pe, wt_done, J)
                        for c in range(CK):
                            last = pe.transpose(p_w[:, c, :], codes_b[:, c * P:(c + 1) * P], identb[:, :])
                        last.then_inc(wtr_done, 1)

            pe.wait_ge(consts, 9)
            for T in range(TPB):
                turn(T, T)
            step(0, True)
            with pe.Fori(1, B - 1) as b:
                step(b, True)
            step(B - 1, False)

        @block.scalar
        def _(act):
            def std(T, t):
                act.wait_ge(ln_aggr, T + 1)
                act.activation(mv[:, t % 2, 2:3], mv[:, t % 2, 1:2], ACT.Sqrt, bias=eps[:, 0:1]).then_inc(ln_std, 1)

            def tr_high(b, T, t):
                for half in range(2):
                    act.wait_ge(tr_done, 2 * T + half + 1)
                    out = xth[:, bass.ds((b % 2) * CK + 4 * half, 4), t * P:(t + 1) * P]
                    act.copy(out, p_tr[half][:, :, :]).then_inc(tr_hi, 1)

            def step(b, more):
                act.wait_ge(kv_done, b + 1)
                at_least(act, vt_done, b)
                at_least(act, k_done, 2 * b)
                act.activation(kt[0:96, :], p_kv[0:96, :], ACT.Copy, scale=SCALE).then_inc(kt_done, 1)
                act.copy(kt[96:P, :], p_kv[96:P, :]).then_inc(kt_done, 1)
                for m in range(CK):
                    n = 8 * b + m
                    if more and m in tile_before:
                        std(4 * b + 4 + tile_before[m], tile_before[m])
                    act.wait_ge(q_done, n + 1)
                    at_least(act, q_out[m % 2], 32 * (4 * b + m // 2))
                    act.copy(qh[:, m % 2, :], p_q[m % 2][:, :]).then_inc(qh_done, 1)
                    if m == 0:
                        act.wait_ge(vt_done, b + 1)
                        act.copy(vst[:, bass.ds(TPB * b, TPB), :], p_vt[:, :, 96:P]).then_inc(v_done, 1)
                    if more and m in tile_after:
                        t = tile_after[m]
                        if t == 0:
                            at_least(act, q_done, 8 * b)
                        tr_high(b + 1, 4 * b + 4 + t, t)
                    if m in codes_after:
                        J = 2 * b + codes_after[m]
                        act.wait_ge(wtr_done, J + 1)
                        at_least(act, wt_out, 16 * J)
                        act.copy(wt[:, :, :], p_w[:, :, :]).then_inc(wt_done, 1)

            act.wait_ge(consts, 6)
            std(0, 0)
            std(1, 1)
            act.wait_ge(kv_in, 16)
            for r in range(4):
                src = raw_kv[:, :, 0:32] if r < 3 else raw_kv[:, :, 32:64]
                act.copy(wkvh[:, :, 32 * r:32 * r + 32], src).then_inc(kv_hi, 1)
            tr_high(0, 0, 0)
            std(2, 2)
            tr_high(0, 1, 1)
            std(3, 3)
            tr_high(0, 2, 2)
            tr_high(0, 3, 3)
            for u in range(8):
                half, c = u // 4, 2 * (u % 4)
                act.wait_ge(raw_in[u % 2], 16 * (u // 2 + 1))
                act.copy(wqh[:, c:c + 2, half * 512:(half + 1) * 512], raw[:, u % 2, :, :]).then_inc(wq_hi, 1)
            step(0, True)
            with act.Fori(1, B - 1) as b:
                step(b, True)
            step(B - 1, False)

        @block.vector
        def _(dve):
            def normalise(T, t):
                dve.wait_ge(x_in[t % 2], 16 * (T // 2 + 1) if isinstance(T, int) else 8 * (T - t % 2) + 16)
                for i in range(2):
                    dve.bn_stats(stats[:, t % 2, i, :], xin[:, t % 2, i * 512:(i + 1) * 512]).then_inc(ln_stats, 1)
                wait_apart(dve, ln_stats, 2 * T + 2, keep["passed"])
                dve.bn_aggr(mv[:, t % 2, 0:2], stats[:, t % 2, :, :].rearrange("p a b -> p (a b)")).then_inc(ln_aggr, 1)
                dve.wait_ge(ln_std, T + 1)
                dve.reciprocal(mv[:, t % 2, 3:4], mv[:, t % 2, 2:3]).then_inc(ln_rstd, 1)
                dve.wait_ge(ln_rstd, T + 1)
                at_least(dve, tr_done, 2 * T - 2)
                dve.tensor_scalar(xn[:, t % 2, :], xin[:, t % 2, :], mv[:, t % 2, 0:1], mv[:, t % 2, 3:4],
                                  ALU.subtract, ALU.mult).then_inc(xn_done, 1)

            def tr_low(b, T, t):
                for half in range(2):
                    dve.wait_ge(tr_hi, 2 * T + half + 1)
                    at = (b % 2) * CK + 4 * half
                    dve.tensor_tensor(xtl[:, bass.ds(at, 4), t * P:(t + 1) * P], p_tr[half][:, :, :],
                                      xth[:, bass.ds(at, 4), t * P:(t + 1) * P], ALU.subtract).then_inc(tr_lo, 1)

            def unpack(J):
                dve.wait_ge(qw_in, 16 * J + 16)
                at_least(dve, codes_done, J)
                dve.tensor_scalar(codes[:, :, 0], qw[:, :, 0], 63, None, ALU.bitwise_and).then_inc(unpacked, 1)
                dve.tensor_scalar(codes[:, :, 1], qw[:, :, 0], 6, 63, ALU.logical_shift_right, ALU.bitwise_and).then_inc(unpacked, 1)
                dve.tensor_scalar(codes[:, :, 2], qw[:, :, 1], 63, None, ALU.bitwise_and).then_inc(unpacked, 1)
                dve.tensor_scalar(codes[:, :, 3], qw[:, :, 2], 63, None, ALU.bitwise_and).then_inc(unpacked, 1)
                dve.wait_ge(unpacked, 4 * J + 4)
                at_least(dve, wtr_done, J)
                dve.tensor_scalar(codes_b[:, :], codes[:, :, :].rearrange("p g i -> p (g i)"), ZERO_CODE, None,
                                  ALU.subtract).then_inc(codes_done, 1)

            def step(b, more):
                cols = bass.ds(b * S, S)
                dve.wait_ge(kt_done, 2 * b + 1)
                dve.tensor_copy(kst[0:96, cols], kt[0:96, :]).then_inc(k_done, 1)
                dve.wait_ge(k_done, 2 * b + 1)
                dve.tensor_tensor(kst[64:96, cols], kt[64:96, :], kst[64:96, cols], ALU.subtract).then_inc(k_done, 1)
                for m in range(CK):
                    n = 8 * b + m
                    if more and m in tile_before:
                        normalise(4 * b + 4 + tile_before[m], tile_before[m])
                    if m in (2, 6):
                        unpack(2 * b + m // 4)
                    dve.wait_ge(qh_done, n + 1)
                    at_least(dve, q_out[m % 2], 32 * (4 * b + m // 2))
                    dve.tensor_tensor(ql[:, m % 2, :], p_q[m % 2][:, :], qh[:, m % 2, :], ALU.subtract).then_inc(q_freed, 1)
                    if more and m in tile_after:
                        tr_low(b + 1, 4 * b + 4 + tile_after[m], tile_after[m])

            dve.memset(mv[:, :, :], 0.0).then_inc(q_freed, 2)
            dve.wait_ge(q_freed, 2)
            normalise(0, 0)
            normalise(1, 1)
            dve.wait_ge(kv_in, 16)
            for r in range(4):
                src = raw_kv[:, :, 0:32] if r < 3 else raw_kv[:, :, 32:64]
                dve.wait_ge(kv_hi, r + 1)
                dve.tensor_tensor(wkvl[:, :, 32 * r:32 * r + 32], src, wkvh[:, :, 32 * r:32 * r + 32], ALU.subtract).then_inc(kv_lo, 1)
            tr_low(0, 0, 0)
            normalise(2, 2)
            tr_low(0, 1, 1)
            normalise(3, 3)
            tr_low(0, 2, 2)
            tr_low(0, 3, 3)
            dve.wait_ge(slopes_in, 16)
            dve.tensor_copy(slopes_r[:, :], slopes_raw[:, :]).then_inc(slopes_rounded, 1)
            dve.wait_ge(kpos_in, 16)
            for i in range(B):
                dve.tensor_copy(kst[R_BIAS:R_END, i * S:(i + 1) * S], kpos_raw[R_BIAS:R_END, :]).then_inc(keep["kst_ext"], 1)
            for u in range(8):
                half, c = u // 4, 2 * (u % 4)
                dve.wait_ge(wq_hi, u + 1)
                at = (slice(None), slice(c, c + 2), slice(half * 512, (half + 1) * 512))
                dve.tensor_tensor(wql[at], raw[:, u % 2, :, :], wqh[at], ALU.subtract).then_inc(wq_lo, 1)
            step(0, True)
            with dve.Fori(1, B - 1) as b:
                step(b, True)
            step(B - 1, False)


def attend(nc, wo, qh_d, ql_d, ext_d, keep, ot, wo_raw):
    AHEAD = 7
    STEPS = GROUPS * B
    ident, identb, kst, vst, ones, mask, future = (
        keep[n] for n in ("ident", "identb", "kst", "vst", "ones", "mask", "future"))
    with ExitStack() as ctx:
        def sb(name, shape, dt=F32):
            return ctx.enter_context(nc.sbuf_tensor(name, shape, dt))

        def psum(name, shape, dt=F32):
            return ctx.enter_context(nc.psum_tensor(name, shape, dt))

        def sem(name):
            return ctx.enter_context(nc.semaphore(name))

        qst = [sb(f"qst{i}", [P, 4 * S], F32R) for i in range(4)]
        pt = [sb(f"pt{i}", [P, 4, PT_COLS]) for i in range(2)]
        mx = [sb(f"mx{i}", [P, P]) for i in range(2)]
        mh, ml = sb("mh", [16, 2, P], F32R), sb("ml", [16, 2, P], F32R)
        spill = sb("spill", [P, 4, S], BF16)
        sums_t = sb("sums_t", [P, 16, 32])
        inv = sb("inv", [P, 16])
        inv_t = sb("inv_t", [P, S])
        o_raw = sb("o_raw", [P, S])

        p_s = [psum(f"p_s{i}", [P, S]) for i in range(2)]
        p_st = psum("p_st", [P, 3 * S])
        p_o, p_sum = psum("p_o", [P, S]), psum("p_sum", [P, S])
        p_m = psum("p_m", [P, S])

        wo_in = keep["wo_in"]
        q_in = [sem(f"q_in{i}") for i in range(4)]
        m_in = [sem(f"m_in{i}") for i in range(2)]
        mx_clear = sem("mx_clear")
        s_done, max_done, mt_done, mh_done, ml_done = (sem(n) for n in ("s_done", "max_done", "mt_done", "mh_done", "ml_done"))
        st_done, exp_done, pv_done = sem("st_done"), sem("exp_done"), sem("pv_done")
        o_taken = sem("o_taken")
        sums_turned, inv_done, inv_turned, norm_done = (sem(n) for n in ("sums_turned", "inv_done", "inv_turned", "norm_done"))

        def loop(eng, step):
            step(0)
            with eng.Fori(1, GROUPS - 1) as g:
                step(g)
            step(GROUPS - 1)

        def later(g, b, j, by):
            off = 4 * b + j + by
            if isinstance(g, int) and g + off // 16 >= GROUPS:
                return None
            return g + off // 16, off % 16 // 4, off % 4

        block = ctx.enter_context(nc.Block("attend"))

        @block.sync
        def _(sp):
            def load_q(g, b):
                rows, cols = bass.ds(P * g, P), slice(b * S, (b + 1) * S)
                for r, src in enumerate((qh_d, ql_d, qh_d)):
                    sp.dma_start(qst[b][32 * r:32 * r + 32, :].bitcast(F32).rearrange("d (j q) -> d j q", j=4),
                                 src[rows, cols].rearrange("(j d) q -> d j q", j=4)).then_inc(q_in[b], 16)
                sp.dma_start(qst[b][R_BIAS:R_MAX, :].bitcast(F32), ext_d[:, bass.ds(4 * S * g, 4 * S)]).then_inc(q_in[b], 16)

            def store_max(s, b):
                sp.wait_ge(ml_done, s + 1)
                for r, src in enumerate((mh, ml)):
                    sp.dma_start(qst[b][R_MAX + r:R_MAX + r + 1, :].bitcast(F32).rearrange("a (n q) -> a n q", n=16),
                                 src[:, b % 2, :].bitcast(F32)).then_inc(m_in[b % 2], 16)

            def step(g):
                for b in range(B):
                    s = B * g + b
                    ahead = later(g, b, 0, 12)
                    if ahead:
                        at_least(sp, st_done, 4 * s)
                        load_q(*ahead[:2])
                    follows = later(g, b, 0, 4)
                    if follows:
                        store_max(s + 1, follows[1])

            for b in range(3):
                load_q(0, b)
            store_max(0, 0)
            sp.dma_start(wo_raw[:, :, :], wo.rearrange("(c p) n -> p c n", p=P)).then_inc(wo_in, 16)
            loop(sp, step)

        @block.tensor
        def _(pe):
            def scores(g, b, j, blocks=range(4)):
                if j == 0 and 0 in blocks:
                    pe.wait_ge(q_in[b], 64 * g + 64)
                for qb in blocks:
                    n = 4 * (16 * g + 4 * b + j) + qb
                    at_least(pe, max_done, n - 1)
                    q0, keys = j * S + qb * P, (qb + 1) * P
                    pe.matmul(p_s[qb % 2][:, 0:keys], qst[b][0:R_MAX, q0:q0 + P], kst[0:R_MAX, b * S:b * S + keys],
                              start=True, stop=True).then_inc(s_done, 1)

            def turn_max(s, b):
                pe.wait_ge(max_done, 16 * s + 16)
                at_least(pe, ml_done, s)
                pe.transpose(p_m[:, 0:P], mx[b % 2][:, :], ident[:, :]).then_inc(mt_done, 1)

            def scores_t(g, b, j):
                i = 16 * g + 4 * b + j
                if j == 0:
                    pe.wait_ge(m_in[b % 2], 32 * (2 * g + b // 2) + 32)
                at_least(pe, exp_done, i)
                for kb in range(4):
                    pe.matmul(p_st[:, KB_AT[kb]:KB_AT[kb] + KB_LEN[kb]],
                              kst[0:R_END, b * S + kb * P:b * S + (kb + 1) * P],
                              qst[b][0:R_END, j * S + kb * P:(j + 1) * S], start=True, stop=False,
                              skip_group_check=True)
                    last = pe.matmul(p_st[:, KB_AT[kb]:KB_AT[kb] + P], identb[:, :], future[:, :],
                                     start=False, stop=True, skip_group_check=True)
                last.then_inc(st_done, 1)

            def values(s, b, part):
                if part == 0:
                    pe.wait_ge(exp_done, 4 * s + 4)
                    at_least(pe, o_taken, s)
                if part == 1:
                    at_least(pe, sums_turned, s)
                for kb, out, w in PARTS[part]:
                    for h in range(4):
                        last = pe.matmul(out[32 * h:32 * h + 32, kb * P:S],
                                         ones[:, :] if w is ones else w[:, TPB * b + kb, :],
                                         pt[b % 2][:, h, KB_AT[kb]:KB_AT[kb] + KB_LEN[kb]],
                                         start=(kb == 0), stop=(kb == 3), tile_position=(0, 32 * h),
                                         skip_group_check=True)
                if part == len(PARTS) - 1:
                    last.then_inc(pv_done, 1)

            PARTS = [[(0, p_o, vst)], [(0, p_sum, ones)], [(1, p_o, vst)], [(1, p_sum, ones)],
                     [(2, p_o, vst), (3, p_o, vst)], [(2, p_sum, ones), (3, p_sum, ones)]]

            def step(g):
                for b in range(B):
                    s = B * g + b
                    earlier = not (isinstance(s, int) and s == 0)
                    for j in range(4):
                        scores_t(g, b, j)
                        ahead = later(g, b, j, AHEAD)
                        if ahead:
                            scores(*ahead, blocks=(0, 1))
                        if j >= 1 and earlier:
                            values(s - 1, (b - 1) % B, 2 * j - 2)
                        if j == 1 and later(g, b, 0, 4):
                            turn_max(s + 1, (b + 1) % B)
                        if ahead:
                            scores(*ahead, blocks=(2, 3))
                        if j >= 1 and earlier:
                            values(s - 1, (b - 1) % B, 2 * j - 1)

            pe.wait_ge(mx_clear, 2)
            for i in range(AHEAD):
                scores(0, i // 4, i % 4)
                if i == 3:
                    turn_max(0, 0)
            loop(pe, step)
            for part in range(len(PARTS)):
                values(STEPS - 1, B - 1, part)

        @block.scalar
        def _(act):
            def max_high(s, b):
                act.wait_ge(mt_done, s + 1)
                at_least(act, m_in[b % 2], 32 * (s // 2) if isinstance(s, int) else 16 * (s - b % 2))
                act.activation(mh[:, b % 2, :], p_m[0:16, 0:P], ACT.Copy, scale=-1.0).then_inc(mh_done, 1)

            def take_o(s):
                act.wait_ge(pv_done, s + 1)
                at_least(act, norm_done, s)
                act.copy(o_raw[:, :], p_o[:, :]).then_inc(o_taken, 1)

            def step(g):
                for b in range(B):
                    s = B * g + b
                    for j in range(4):
                        i = 16 * g + 4 * b + j
                        if j == 0 and not (isinstance(s, int) and s < 2):
                            take_o(s - 2)
                        act.wait_ge(st_done, i + 1)
                        if j == 0:
                            at_least(act, pv_done, s - 1)
                        act.activation(pt[b % 2][:, j, :], p_st[:, 0:PT_COLS], ACT.Exp).then_inc(exp_done, 1)
                        if j == 1 and later(g, b, 0, 4):
                            max_high(s + 1, (b + 1) % B)

            max_high(0, 0)
            loop(act, step)
            take_o(STEPS - 2)
            take_o(STEPS - 1)

        @block.gpsimd
        def _(pool):
            for m in mx:
                pool.memset(m[:, :], 0.0).then_inc(mx_clear, 1)

        @block.vector
        def _(dve):
            def maxima(g, b, j, blocks=range(4)):
                s = B * g + b
                if j == 0 and 0 in blocks:
                    at_least(dve, mt_done, s - 1)
                for qb in blocks:
                    n = 16 * s + 4 * j + qb
                    if not (isinstance(n, int) and n < 4):
                        dve.wait_ge(max_done, n - 3)
                    wait_apart(dve, s_done, n + 1, keep["passed"])
                    keys = (qb + 1) * P
                    dve.tensor_tensor_reduce(spill[:, qb, 0:keys], p_s[qb % 2][:, 0:keys], mask[:, S - keys:S], 1.0,
                                             LOWEST, ALU.add, ALU.max,
                                             mx[b % 2][:, 4 * j + qb:4 * j + qb + 1]).then_inc(max_done, 1)

            def max_low(s, b):
                dve.wait_ge(mh_done, s + 1)
                at_least(dve, m_in[b % 2], 32 * (s // 2) if isinstance(s, int) else 16 * (s - b % 2))
                dve.scalar_tensor_tensor(out=ml[:, b % 2, :], in0=p_m[0:16, 0:P], scalar=-1.0, in1=mh[:, b % 2, :],
                                         op0=ALU.mult, op1=ALU.subtract).then_inc(ml_done, 1)

            def normalise(s, g, b, part):
                if part == 0:
                    dve.wait_ge(pv_done, s + 1)
                    dve.transpose(sums_t[:, :, :].rearrange("p n r -> p (n r)"), p_sum[:, :]).then_inc(sums_turned, 1)
                if part == 1:
                    dve.wait_ge(sums_turned, s + 1)
                    dve.reciprocal(inv[:, :], sums_t[:, :, 0]).then_inc(inv_done, 1)
                if part == 2:
                    dve.wait_ge(inv_done, s + 1)
                    dve.transpose(inv_t[:, :], inv[:, :, None].to_broadcast([P, 16, 32])).then_inc(inv_turned, 1)
                if part == 3:
                    dve.wait_ge(inv_turned, s + 1)
                    dve.wait_ge(o_taken, s + 1)
                    dve.tensor_tensor(ot[:, b * TPB:(b + 1) * TPB, bass.ds(g, 1), :].rearrange("p t g q -> p t (g q)"),
                                      o_raw[:, :].rearrange("p (t q) -> p t q", t=TPB),
                                      inv_t[:, :].rearrange("p (t q) -> p t q", t=TPB), ALU.mult).then_inc(norm_done, 1)

            def step(g):
                for b in range(B):
                    s = B * g + b
                    done = () if isinstance(s, int) and s < 2 else (s - 2, g if b >= 2 else g - 1, (b - 2) % B)
                    for j in range(4):
                        if done and j == 0:
                            normalise(*done, 0)
                        if done and j == 2:
                            normalise(*done, 3)
                        ahead = later(g, b, j, AHEAD)
                        if ahead:
                            maxima(*ahead, blocks=(0, 1))
                        if done and j == 0:
                            normalise(*done, 1)
                        if done and j == 1:
                            normalise(*done, 2)
                        if ahead:
                            maxima(*ahead, blocks=(2, 3))
                        if j == 1 and later(g, b, 0, 4):
                            max_low(s + 1, (b + 1) % B)

            dve.wait_ge(mx_clear, 2)
            for i in range(AHEAD):
                maxima(0, i // 4, i % 4)
                if i == 3:
                    max_low(0, 0)
            loop(dve, step)
            for s in (STEPS - 2, STEPS - 1):
                for part in range(4):
                    normalise(s, s // B, s % B, part)


def split_wo(nc, keep, wo_raw, woh, wol):
    with ExitStack() as ctx:
        wo_hi, wo_lo = (ctx.enter_context(nc.semaphore(n)) for n in ("wo_hi", "wo_lo"))
        block = ctx.enter_context(nc.Block("split_wo"))

        @block.scalar
        def _(act):
            act.wait_ge(keep["wo_in"], 16)
            for c in range(CK):
                act.copy(woh[:, c, :], wo_raw[:, c, :]).then_inc(wo_hi, 1)

        @block.vector
        def _(dve):
            dve.wait_ge(keep["wo_in"], 16)
            for c in range(CK):
                dve.wait_ge(wo_hi, c + 1)
                dve.tensor_tensor(wol[:, c, :], wo_raw[:, c, :], woh[:, c, :], ALU.subtract).then_inc(wo_lo, 1)


def finish(nc, x, w_scale, w_zero, bias, out, wi_d, keep, ot, woh, wol):
    ident, eps = keep["ident"], keep["eps"]
    with ExitStack() as ctx:
        def sb(name, shape, dt=F32):
            return ctx.enter_context(nc.sbuf_tensor(name, shape, dt))

        def psum(name, shape, dt=F32):
            return ctx.enter_context(nc.psum_tensor(name, shape, dt))

        def sem(name):
            return ctx.enter_context(nc.semaphore(name))

        wi = sb("wi", [P, CK, D], F32R)
        osh, osl = sb("osh", [P, CK, P], F32R), sb("osl", [P, CK, P], F32R)
        yth, ytl = sb("yth", [P, CK, P], F32R), sb("ytl", [P, CK, P], F32R)
        xr = sb("xr", [P, 2, D])
        y = sb("y", [P, D])
        scale_b, shift_b, bias_b = sb("scale_b", [P, D]), sb("shift_b", [P, D]), sb("bias_b", [P, D])
        shift = sb("shift", [P, D])
        stats = sb("stats3", [P, 2, 6])
        mv = sb("mv3", [P, 4])
        ysum = sb("ysum", [P, 2])

        p_wo, p_ff = psum("p_wo", [P, 2, S]), psum("p_ff", [P, 2, S])
        p_tr = [psum(f"p_tr3{i}", [P, 4, P]) for i in range(2)]

        wi_in, rows_in, shift_done = sem("wi_in"), sem("rows_in"), sem("shift_done")
        xr_in = [sem(f"xr_in{i}") for i in range(2)]
        o_hi, o_lo, wo_done, x2_done = (sem(n) for n in ("o_hi", "o_lo", "wo_done", "x2_done"))
        ln_stats, ln_aggr, ln_std, ln_rstd, ln_mean, y_done = (
            sem(n) for n in ("ln_stats3", "ln_aggr3", "ln_std3", "ln_rstd3", "ln_mean3", "y_done"))
        turned, t_hi, t_lo = sem("turned"), sem("t_hi"), sem("t_lo")
        ff_done, scaled, res_bias, res_shift, res_done, out_done, stored = (
            sem(n) for n in ("ff_done", "scaled", "res_bias", "res_shift", "res_done", "out_done", "stored"))

        x_rows, out_rows = x.rearrange("b s d -> (b s) d"), out.rearrange("b s d -> (b s) d")
        LAST = TILES - 1

        def slot(t):
            return bass.ds(t % 2, 1)

        def flat(ap):
            return ap.rearrange("p a n -> p (a n)")

        def o_tile(t):
            return ot[:, bass.ds(t, 1), :, :].rearrange("p a c q -> p (a c q)")

        def loop(eng, step):
            for t in range(2):
                step(t, t, False)
            with eng.Fori(1, TILES // 2 - 1) as k:
                for odd in range(2):
                    step(2 * k + odd, odd, False)
            for t in range(TILES - 2, TILES):
                step(t, t % 2, t == LAST)

        block = ctx.enter_context(nc.Block("finish"))

        @block.sync
        def _(sp):
            def load_x(t, odd):
                sp.dma_start(xr[:, odd, :], x_rows[bass.ds(t * P, P), :]).then_inc(xr_in[odd], 16)

            def step(t, odd, last):
                if not (last or isinstance(t, int) and t == LAST - 1):
                    sp.wait_ge(out_done, t + 1)
                    load_x(t + 2, odd)
                else:
                    sp.wait_ge(out_done, t + 1)
                sp.dma_start(out_rows[bass.ds(t * P, P), :], o_tile(t)).then_inc(stored, 16)

            load_x(0, 0)
            load_x(1, 1)
            for c in range(CK):
                sp.dma_start(wi[:, c, :].bitcast(F32), wi_d[:, c, :]).then_inc(wi_in, 16)
            loop(sp, step)
            sp.wait_ge(stored, 16 * TILES)

        @block.tensor
        def _(pe):
            def out_proj(t):
                pe.wait_ge(o_lo, t + 1)
                at_least(pe, x2_done, t)
                for c in range(CK):
                    for k, (a, w) in enumerate(((osh, woh), (osh, wol), (osl, woh))):
                        for n in range(2):
                            last = pe.matmul(p_wo[:, n, :], a[:, c, :], w[:, c, n * S:(n + 1) * S],
                                             start=(c == 0 and k == 0), stop=(c == CK - 1 and k == 2))
                last.then_inc(wo_done, 1)

            def ffn(t):
                pe.wait_ge(t_lo, 2 * t + 2)
                at_least(pe, scaled, t)
                for c in range(CK):
                    for a in (yth, ytl):
                        for n in range(2):
                            last = pe.matmul(p_ff[:, n, :], a[:, c, :], wi[:, c, n * S:(n + 1) * S],
                                             start=(c == 0 and a is yth), stop=(c == CK - 1 and a is ytl))
                last.then_inc(ff_done, 1)

            def turn(t):
                pe.wait_ge(y_done, t + 1)
                for half in range(2):
                    at_least(pe, t_lo, 2 * t - 1 + half)
                    for i in range(4):
                        c = 4 * half + i
                        last = pe.transpose(p_tr[half][:, i, :], y[:, c * P:(c + 1) * P], ident[:, :])
                    last.then_inc(turned, 1)

            def step(t, odd, last):
                if not last:
                    out_proj(t + 1)
                ffn(t)
                if not last:
                    turn(t + 1)

            out_proj(0)
            turn(0)
            pe.wait_ge(wi_in, 16 * CK)
            loop(pe, step)

        @block.scalar
        def _(act):
            def o_high(t):
                at_least(act, wo_done, t)
                act.copy(osh[:, :, :].rearrange("p c q -> p (c q)"), o_tile(t)).then_inc(o_hi, 1)

            def std_y(t):
                act.wait_ge(ln_aggr, t + 1)
                act.activation(mv[:, 2:3], mv[:, 1:2], ACT.Sqrt, bias=eps[:, 0:1]).then_inc(ln_std, 1)
                act.wait_ge(ln_rstd, t + 1)
                act.wait_ge(ln_mean, t + 1)
                at_least(act, res_shift, t)
                act.activation(y[:, :], y[:, :], ACT.Copy, scale=mv[:, 3:4], accum_out=ysum[:, 0:1]).then_inc(y_done, 1)

            def t_high(t):
                at_least(act, ff_done, t)
                for half in range(2):
                    act.wait_ge(turned, 2 * t + half + 1)
                    act.copy(yth[:, 4 * half:4 * half + 4, :], p_tr[half][:, :, :]).then_inc(t_hi, 1)

            def step(t, odd, last):
                if last:
                    return
                std_y(t + 1)
                if not (isinstance(t, int) and t == LAST - 1):
                    o_high(t + 2)
                t_high(t + 1)

            o_high(0)
            std_y(0)
            o_high(1)
            t_high(0)
            loop(act, step)

        @block.gpsimd
        def _(pool):
            def o_low(t):
                wait_apart(pool, o_hi, t + 1, keep["passed"])
                pool.tensor_tensor(osl[:, :, :].rearrange("p c q -> p (c q)"), o_tile(t),
                                   osh[:, :, :].rearrange("p c q -> p (c q)"), ALU.subtract).then_inc(o_lo, 1)

            def residual(t, odd):
                xt = xr[:, odd, :]
                pool.wait_ge(y_done, t + 1)
                pool.wait_ge(ln_mean, t + 1)
                pool.tensor_tensor(xt, xt, bias_b[:, :], ALU.add).then_inc(res_bias, 1)
                if not (isinstance(t, int) and t == 0):
                    wait_apart(pool, res_done, t, keep["passed"])
                pool.tensor_scalar(shift[:, :], shift_b[:, :], ysum[:, 0:1], None, ALU.mult).then_inc(res_shift, 1)
                pool.wait_ge(res_bias, t + 1)
                pool.wait_ge(res_shift, t + 1)
                pool.tensor_tensor(xt, xt, shift[:, :], ALU.subtract).then_inc(res_done, 1)

            def step(t, odd, last):
                if last:
                    return
                if not (isinstance(t, int) and t == LAST - 1):
                    o_low(t + 2)
                residual(t + 1, 1 - odd)

            for dst, src in ((scale_b, w_scale.rearrange("n a -> a n")), (shift_b, w_zero.rearrange("n a -> a n")),
                             (bias_b, bias.rearrange("(a n) -> a n", a=1))):
                pool.dma_start(dst[:, :], src.to_broadcast([P, D])).then_inc(rows_in, 16)
            o_low(0)
            pool.wait_ge(rows_in, 48)
            pool.tensor_scalar(shift_b[:, :], shift_b[:, :], ZERO_CODE, None, ALU.subtract).then_inc(shift_done, 1)
            pool.wait_ge(shift_done, 1)
            pool.tensor_tensor(shift_b[:, :], shift_b[:, :], scale_b[:, :], ALU.mult).then_inc(shift_done, 1)
            pool.wait_ge(shift_done, 2)
            o_low(1)
            residual(0, 0)
            loop(pool, step)

        @block.vector
        def _(dve):
            def norm(t, odd):
                xt = xr[:, odd, :]
                dve.wait_ge(xr_in[odd], 16 * (t // 2) + 16 if isinstance(t, int) else 8 * (t - odd) + 16)
                dve.wait_ge(wo_done, t + 1)
                dve.tensor_tensor(xt, xt, flat(p_wo[:, :, :]), ALU.add).then_inc(x2_done, 1)
                dve.wait_ge(x2_done, t + 1)
                for i in range(2):
                    dve.bn_stats(stats[:, i, :], xr[:, odd, i * 512:(i + 1) * 512]).then_inc(ln_stats, 1)
                at_least(dve, y_done, t)
                wait_apart(dve, ln_stats, 2 * t + 2, keep["passed"])
                dve.bn_aggr(mv[:, 0:2], stats[:, :, :].rearrange("p a b -> p (a b)")).then_inc(ln_aggr, 1)
                dve.wait_ge(ln_aggr, t + 1)
                at_least(dve, turned, 2 * t)
                dve.tensor_scalar(y[:, :], xt, mv[:, 0:1], None, ALU.subtract).then_inc(ln_mean, 1)
                dve.wait_ge(ln_std, t + 1)
                dve.reciprocal(mv[:, 3:4], mv[:, 2:3]).then_inc(ln_rstd, 1)

            def t_low(t):
                for half in range(2):
                    dve.wait_ge(t_hi, 2 * t + half + 1)
                    part = slice(4 * half, 4 * half + 4)
                    dve.tensor_tensor(ytl[:, part, :], p_tr[half][:, :, :], yth[:, part, :], ALU.subtract).then_inc(t_lo, 1)

            def result(t, odd):
                dve.wait_ge(ff_done, t + 1)
                dve.wait_ge(o_lo, t + 1)
                dve.tensor_tensor(o_tile(t), flat(p_ff[:, :, :]), scale_b[:, :], ALU.mult).then_inc(scaled, 1)
                dve.wait_ge(scaled, t + 1)
                dve.wait_ge(res_done, t + 1)
                dve.tensor_tensor(o_tile(t), o_tile(t), xr[:, odd, :], ALU.add).then_inc(out_done, 1)

            def step(t, odd, last):
                if not last:
                    norm(t + 1, 1 - odd)
                result(t, odd)
                if not last:
                    t_low(t + 1)

            dve.wait_ge(rows_in, 48)
            norm(0, 0)
            t_low(0)
            loop(dve, step)


def build(nc, x, wq, wkv, wo, qweight, w_scale, w_zero, bias, kpos, slopes, out):
    qh_d = nc.dram_tensor("qh_d", [D, ROWS], F32, kind="Internal").ap()
    ql_d = nc.dram_tensor("ql_d", [D, ROWS], F32, kind="Internal").ap()
    ext_d = nc.dram_tensor("ext_d", [2, HEADS * S], F32, kind="Internal").ap()
    wi_d = nc.dram_tensor("wi_d", [P, CK, D], F32, kind="Internal").ap()
    with ExitStack() as ctx:
        keep = {
            "ident": ctx.enter_context(nc.sbuf_tensor("ident", [P, P], F32)),
            "eps": ctx.enter_context(nc.sbuf_tensor("eps", [P, 1], F32)),
            "kst_ext": ctx.enter_context(nc.semaphore("kst_ext")),
            "passed": ctx.enter_context(nc.semaphore("passed")),
            "wo_in": ctx.enter_context(nc.semaphore("wo_in")),
        }
        with ExitStack() as heads:
            keep["kst"] = heads.enter_context(nc.sbuf_tensor("kst", [P, ROWS], F32R))
            keep["vst"] = heads.enter_context(nc.sbuf_tensor("vst", [P, TILES, HD], F32))
            keep["ones"] = heads.enter_context(nc.sbuf_tensor("ones", [P, HD], F32))
            keep["identb"] = heads.enter_context(nc.sbuf_tensor("identb", [P, P], BF16))
            keep["future"] = heads.enter_context(nc.sbuf_tensor("future", [P, P], BF16))
            keep["mask"] = heads.enter_context(nc.sbuf_tensor("mask", [P, S], F32))
            project(nc, x, wq, wkv, qweight, kpos, slopes, qh_d, ql_d, ext_d, wi_d, keep)
            ot = ctx.enter_context(nc.sbuf_tensor("ot", [P, TILES, CK, P], F32, side="right"))
            raw = ExitStack()
            wo_raw = raw.enter_context(nc.sbuf_tensor("wo_raw", [P, CK, D], F32, side="right"))
            attend(nc, wo, qh_d, ql_d, ext_d, keep, ot, wo_raw)
        woh = ctx.enter_context(nc.sbuf_tensor("woh", [P, CK, D], F32R))
        wol = ctx.enter_context(nc.sbuf_tensor("wol", [P, CK, D], F32R))
        split_wo(nc, keep, wo_raw, woh, wol)
        raw.close()
        finish(nc, x, w_scale, w_zero, bias, out, wi_d, keep, ot, woh, wol)


def slope_table():
    start = 2.0 ** (-2.0 ** (-(np.log2(HEADS) - 3)))
    slopes = np.array([start ** (i + 1) for i in range(HEADS)], dtype=np.float32)
    high = (slopes.view(np.uint32) & np.uint32(0xFFFFF000)).view(np.float32)
    return np.ascontiguousarray(np.broadcast_to(np.stack([high, slopes - high])[:, :, None], (2, HEADS, S)))


def position_table():
    where = np.arange(S, dtype=np.float32) - np.float32(S // 2)
    one = np.ones(S, dtype=np.float32)
    return np.stack([where, where, one, one])


def kernel(L0_attn_hidden_states, L0_attn_Wq, L0_attn_Wkv, L0_attn_Wo, L0_ffn_qweight, L0_ffn_weight_scale,
           L0_ffn_weight_zero_point, L0_ffn_bias):
    import concourse.bacc as _bacc
    from concourse.bass_utils import run_bass_kernel_spmd as _run

    nc = _bacc.Bacc("TRN2", target_bir_lowering=False, num_devices=1)
    given = {
        "x": L0_attn_hidden_states, "wq": L0_attn_Wq, "wkv": L0_attn_Wkv, "wo": L0_attn_Wo,
        "qweight": L0_ffn_qweight, "w_scale": L0_ffn_weight_scale, "w_zero": L0_ffn_weight_zero_point,
        "bias": L0_ffn_bias, "kpos": position_table(), "slopes": slope_table(),
    }
    arrays, args = {}, []
    for name, value in given.items():
        a = np.ascontiguousarray(value)
        arrays[f"in_{name}_dram"] = a
        args.append(nc.dram_tensor(f"in_{name}_dram", a.shape, mybir.dt.from_np(a.dtype), kind="ExternalInput").ap())
    out = nc.dram_tensor("out_dram", (B, S, D), F32, kind="ExternalOutput").ap()
    build(nc, *args, out)
    r = _run(nc, [arrays], core_ids=[0])
    return r.results[0]["out_dram"]
```
